# Optimizing a Trainium2 kernel written in Bass

```python
import numpy as np
import jax
import jax.numpy as jnp

def _softmax(x, axis=-1):
    return jax.nn.softmax(x, axis=axis)

def _gelu(x):
    return jax.nn.gelu(x, approximate=True)

def _silu(x):
    return jax.nn.silu(x)

def _sigmoid(x):
    return jax.nn.sigmoid(x)

def _layernorm(x, axis=-1, eps=1e-05):
    m = jnp.mean(x, axis=axis, keepdims=True)
    v = jnp.var(x, axis=axis, keepdims=True)
    return (x - m) / jnp.sqrt(v + eps)

def _scatter_add(tgt, idx, src, axis=0):
    return tgt.at[idx].add(src)

def _segment_sum(src, seg, n):
    return jax.ops.segment_sum(src, seg, n)
kernel_name = 'mk_adj_preln_d1_adj_r2_a7ce50'

def setup_inputs(seed: int=0):
    np.random.seed(seed)
    _w = jnp.asarray

    def _rec_inputs():
        import jax
        import jax.numpy as jnp
        _gk = jax.random.key(seed)
        x = -0.0005207 + 1.001 * jax.random.normal(jax.random.fold_in(_gk, 1), (8192, 128), jnp.float32)
        _w = (1.0 + jnp.arange(8192, dtype=jnp.float32)) ** (-0.5)
        _w = _w / _w.mean()
        _pij = jnp.clip(0.000488281 * _w[:, None] * _w[None, :], 0.0, 1.0)
        _a = jax.random.uniform(jax.random.fold_in(_gk, 2), (8192, 8192)) < _pij
        _a = jnp.logical_or(_a, jnp.eye(8192, dtype=bool))
        _af = _a.astype(jnp.float32)
        _af = _af * jax.random.uniform(jax.random.fold_in(_gk, 3), (8192, 8192), jnp.float32, 0.05, 1)
        adj = _af
        return (x, adj)
    x, adj = _rec_inputs()

    def _L0_gnn_setup():
        import jax, jax.numpy as jnp
        import numpy as np
        N = 4096
        D_IN = 128
        D_OUT = 128
        key = jax.random.key(seed)
        k1, k2, k3 = jax.random.split(key, 3)
        x = jax.random.normal(k1, (N, D_IN), dtype=jnp.float32)
        adj = jax.random.uniform(k2, (N, N), dtype=jnp.float32)
        W = jax.random.normal(k3, (D_OUT, D_IN), dtype=jnp.float32) * (1.0 / np.sqrt(D_IN))
        return {'x': x, 'adj': adj, 'W': W}
    _L0_gnn_all = _L0_gnn_setup()
    _L0_gnn_in = {k: v for k, v in _L0_gnn_all.items() if k in ('W',)}
    del _L0_gnn_all
    return {'x': x, 'adj': adj, 'L0_gnn_W': _L0_gnn_in['W']}

def reference(x, adj, L0_gnn_W):
    import jax
    import jax.numpy as jnp

    def _L0_gnn_ref(x, adj, W):
        import jax, jax.numpy as jnp
        import numpy as np
        N = 4096
        D_IN = 128
        D_OUT = 128
        A_hat = adj + jnp.eye(adj.shape[0], dtype=adj.dtype)
        d_inv_sqrt = jnp.sum(A_hat, axis=1) ** (-0.5)
        A_norm = d_inv_sqrt[:, None] * A_hat * d_inv_sqrt[None, :]
        support = x @ W.T
        out = A_norm @ support
        return jax.nn.relu(out)
    h = jnp.maximum(_layernorm(x, axis=-1), 0.0)
    x = x + _L0_gnn_ref(h, adj, L0_gnn_W)
    return x

_drawn_inputs = setup_inputs


def setup_inputs(seed=0):
    import zlib

    import numpy as np

    out = dict(_drawn_inputs(seed))
    spreads = {}
    factors = {}
    for name, (base, spread) in spreads.items():
        noise = np.random.default_rng([zlib.crc32(name.encode()), seed]).standard_normal(out[name].shape)
        drawn = base * np.exp(spread * noise) if base else spread * noise
        out[name] = jnp.asarray(drawn.astype(out[name].dtype))
    for name, factor in factors.items():
        out[name] = (out[name] * factor).astype(out[name].dtype)
    return out
```

```python
import concourse.bass as bass
from concourse import mybir
from contextlib import ExitStack

F32 = mybir.dt.float32
F32R = mybir.dt.float32r
ALU = mybir.AluOpType
ACT = mybir.ActivationFunctionType
AXX = mybir.AxisListType.X

P = 128
SUB = 4
B = P * SUB
LEAD = 2
BAND = 2
SLOTS = 10
NPT = 3
NAT = 4
NACC = BAND + 2
AHEAD = 2


class Plan:

    def __init__(self, groups):
        self.groups = groups
        self.loads, self.units, events = [], [], []
        at, where, arrived = 0.0, {}, []

        def event(pos, *what):
            events.append((pos, len(events), what))

        def load(i, j, summed, used):
            arrived.append(len(self.loads) + 1.0)
            self.loads.append((i, j, summed, used))
            return len(self.loads) - 1

        def products(blocks, start, span):
            nonlocal at
            n = len(blocks) * SUB
            for q in range(n):
                i, j = blocks[q // SUB]
                m = where[i, j]
                at = max(at, start + span * q / n, arrived[m])
                event(at, "unit", len(self.units))
                self.units.append((m, i, j, q % SUB))
                if q % SUB == SUB - 1:
                    if j == min(i + BAND, groups - 1):
                        event(at, "park", i)

        for g in range(groups):
            held = [(i, g - 1) for i in range(max(0, g - 1 - BAND), g)] if g else []
            left = [(g, j) for j in range(g)]
            far = [(g, j) for j in range(g + BAND + 1, groups)]
            near = [(g, j) for j in range(min(g + BAND, groups - 1), g - 1, -1)]
            key = {b: (m - 1 if m < LEAD else len(held) + m - 1) / (len(held) + len(left))
                   for m, b in enumerate(left)}
            key |= {b: (m + 0.5) / len(far) for m, b in enumerate(far)}
            for b in sorted(key, key=key.get) + near:
                where[b] = load(*b, True, b not in far)
                for s in range(SUB):
                    event(arrived[-1] + s / SUB, "sum", where[b], s)
            start = g * groups + 1.0
            for k, what in enumerate(("normalise", "hidden", "turn", "turned", "project", "raw")):
                event(start + 3 + k, what, g)
            lead = left[:min(LEAD, g - 1)] if g > 1 else []
            products(lead + held + left[len(lead):], start + 0.1, groups - 0.2)
            event((g + 1) * groups + 1.0, "scale", g)
        g = groups
        start = g * groups + 1.0
        products([(i, g - 1) for i in range(max(0, g - 1 - BAND), g)], start + 1.2, SUB)
        done = []
        for i in range(groups - BAND - 1):
            blocks = [(i, j) for j in range(i + BAND + 1, groups)]
            for b in blocks:
                where[b] = load(*b, False, True)
            products(blocks, at, len(blocks))
            event(at, "gather", i)
            done.append((at, i))
        rest = [i for i in range(groups - BAND - 1, groups)]
        for i in rest:
            pos = start + 8 + 2 * (i - rest[0])
            event(pos, "gather", i)
            done.append((pos, i))
        for pos, i in done:
            event(pos + 1, "turn out", i)
            event(pos + 2, "finish", i)
            event(pos + 4, "store", i)
        self.timeline = [what for _, _, what in sorted(events)]

        last_use, first = {}, {}
        for pos, e in enumerate(self.timeline):
            m = e[1] if e[0] == "sum" else self.units[e[1]][0] if e[0] == "unit" else None
            if m is not None:
                last_use[m] = pos
        holds = [None] * SLOTS
        self.slots, self.evicted = [], []
        for n in range(len(self.loads)):
            s = min(range(SLOTS), key=lambda s: (-1, s) if holds[s] is None else (last_use[holds[s]], s))
            self.slots.append(s)
            self.evicted.append(holds[s])
            holds[s] = n


def sums_on_act(n, s):
    return s % 2 == 0


def gcn_kernel(nc, x, adj, w, out):
    N, D = x.shape
    G = N // B
    EPS = 1e-5
    plan = Plan(G)
    units, timeline = plan.units, plan.timeline

    x_v = x.rearrange("(g s p) d -> g p s d", s=SUB, p=P)
    out_v = out.rearrange("(g s p) d -> g p s d", s=SUB, p=P)
    adj_v = adj.rearrange("(g s p) c -> g p s c", s=SUB, p=P)

    ctx = ExitStack()
    with ctx:
        def sb(name, shape, dt=F32):
            return ctx.enter_context(nc.sbuf_tensor(name, shape, dt))

        def pb(name):
            return ctx.enter_context(nc.psum_tensor(name, [P, B], F32))

        def sem(name):
            return ctx.enter_context(nc.semaphore(name))

        A = [sb(f"A{r}", [P, SUB, B]) for r in range(SLOTS)]
        Ah = [sb(f"Ah{r}", [P, B], F32R) for r in range(NAT)]
        Al = [sb(f"Al{r}", [P, B], F32R) for r in range(NAT)]
        Sh = sb("Sh", [P, G, SUB, D], F32R)
        Sl = sb("Sl", [P, G, SUB, D], F32R)
        parked = sb("parked", [P, G, B])
        partial = sb("partial", [P, G, SUB, G])
        degree = sb("degree", [P, G, SUB])
        factor = sb("factor", [P, G, SUB])
        minus_half = sb("minus_half", [P, SUB])
        ident = sb("ident", [P, P])
        w_rows = sb("w_rows", [P, D])
        wT = sb("wT", [P, P])
        xg = sb("xg", [P, SUB, D])
        h = sb("h", [P, SUB, D])
        hT = sb("hT", [P, B])
        raw = sb("raw", [P, SUB, D])
        scaled = sb("scaled", [P, SUB, D])
        stats = sb("stats", [P, SUB, 6])
        moments = sb("moments", [P, SUB, 2])
        variance = sb("variance", [P, SUB])
        minus_mean = sb("minus_mean", [P, SUB])
        rstd = sb("rstd", [P, SUB])
        shift = sb("shift", [P, SUB])
        junk = sb("junk", [P, 2, B], mybir.dt.bfloat16)
        total, fin, x_out = hT, (scaled, h), (xg, raw)

        pt = [pb(f"pt{r}") for r in range(NPT)]
        acc = [pb(f"acc{r}") for r in range(NACC)]
        aux = pb("aux")

        block_in = [sem(f"block_in{r}") for r in range(SLOTS)]
        w_in = sem("w_in")
        x_in = sem("x_in")
        x_out_in = [sem(f"x_out_in{r}") for r in range(2)]
        stored = [sem(f"stored{r}") for r in range(2)]
        ident_ready = sem("ident_ready")
        consts_ready = sem("consts_ready")
        wT_made = sem("wT_made")
        wT_ready = sem("wT_ready")
        eye_added = sem("eye_added")
        transposed = sem("transposed")
        high_ready = sem("high_ready")
        low_ready = sem("low_ready")
        multiplied = sem("multiplied")
        act_summed = sem("act_summed")
        dve_summed = sem("dve_summed")
        parked_ready = sem("parked_ready")
        stats_ready = sem("stats_ready")
        moments_ready = sem("moments_ready")
        var_ready = sem("var_ready")
        rstd_ready = sem("rstd_ready")
        shift_ready = sem("shift_ready")
        h_ready = sem("h_ready")
        h_turned = sem("h_turned")
        hT_ready = sem("hT_ready")
        projected = sem("projected")
        raw_ready = sem("raw_ready")
        degree_ready = sem("degree_ready")
        factor_ready = sem("factor_ready")
        scaled_ready = sem("scaled_ready")
        sh_ready = sem("sh_ready")
        s_ready = sem("s_ready")
        total_ready = sem("total_ready")
        out_turned = sem("out_turned")
        relu_ready = sem("relu_ready")
        fin_ready = sem("fin_ready")

        act_sum_no, dve_sum_no = {}, {}
        for e in timeline:
            if e[0] == "sum":
                to = act_sum_no if sums_on_act(*e[1:]) else dve_sum_no
                to[e[1:]] = len(to) + 1
        act_sums_by, dve_sums_by, diagonal_by = {}, {}, {}
        for (n, s), k in act_sum_no.items():
            act_sums_by[n] = k
        for (n, s), k in dve_sum_no.items():
            dve_sums_by[n] = k
        group_of = [i for i, _, _, _ in plan.loads]
        last_unit = {}
        for k, (n, i, j, t) in enumerate(units):
            last_unit[n] = k
        uses = []
        for n in range(len(plan.loads)):
            m = plan.evicted[n]
            uses.append(1 if m is None else uses[m] + 1)
        parks = [e[1] for e in timeline if e[0] == "park"]
        gathers = [e[1] for e in timeline if e[0] == "gather"]
        rereads = G - BAND - 1

        def first_of_run(k):
            return k == 0 or units[k][1] != units[k - 1][1]

        opened = {}
        bank_of = []
        user, emptied, seen = [None] * NACC, [0] * NACC, 0
        open_bank = {}
        second = set()
        ends = {}
        for e in timeline:
            if e[0] == "unit":
                k = e[1]
                i = units[k][1]
                if i not in open_bank:
                    b = i % NACC
                    opened[k] = emptied[b]
                    open_bank[i] = b
                bank_of.append(open_bank[i])
                ends[i] = k
            elif e[0] == "park" or (e[0] == "gather" and e[1] < rereads):
                seen += 1
                emptied[open_bank.pop(e[1])] = seen
        bank_last = set()
        tail = {}
        for k, u in enumerate(units):
            i = u[1]
            phase = plan.loads[u[0]][2]
            tail[i, phase] = k
        bank_last = set(tail.values())
        row_end = tail

        def gather_no(m):
            return gathers.index([i for i in gathers if i < rereads][m - 1]) + 1

        def block_there(eng, n):
            eng.wait_ge(block_in[plan.slots[n]], 16 * uses[n])

        block = ctx.enter_context(nc.Block())

        @block.sync
        def _(sp):
            sp.dma_start(w_rows[:], w[:, :]).then_inc(w_in, 16)
            sp.dma_start(xg[:], x_v[0]).then_inc(x_in, 16)
            for n, (i, j, summed, used) in enumerate(plan.loads):
                if summed and n % G == G // 2 and n // G + 1 < G:
                    g = n // G + 1
                    sp.wait_ge(h_ready, g)
                    sp.dma_start(xg[:], x_v[g]).then_inc(x_in, 16)
                m = plan.evicted[n]
                if m is not None:
                    if m in act_sums_by:
                        sp.wait_ge(act_summed, act_sums_by[m])
                    if m in dve_sums_by:
                        sp.wait_ge(dve_summed, dve_sums_by[m])
                    if m in last_unit:
                        sp.wait_ge(transposed, last_unit[m] + 1)
                sp.dma_start(A[plan.slots[n]][:], adj_v[i][:, :, j * B:(j + 1) * B]).then_inc(
                    block_in[plan.slots[n]], 16)

        @block.gpsimd
        def _(pool):
            nc.gpsimd.memset(ident[:], 0.0).then_inc(consts_ready, 1)
            pool.wait_ge(consts_ready, 1)
            nc.gpsimd.affine_select(out=ident[:], in_=ident[:], compare_op=ALU.not_equal, fill=1.0, base=0,
                                    pattern=[[-1, P]], channel_multiplier=1).then_inc(ident_ready, 1)
            nc.gpsimd.memset(minus_half[:], -0.5).then_inc(consts_ready, 1)
            pool.wait_ge(ident_ready, 1)
            pool.wait_ge(consts_ready, 2)
            eyes, fins = 0, 0
            for e in timeline:
                if e[0] == "sum" and plan.loads[e[1]][0] == plan.loads[e[1]][1]:
                    n, s = e[1:]
                    block_there(pool, n)
                    tile = A[plan.slots[n]][:, s, s * P:(s + 1) * P]
                    nc.gpsimd.tensor_tensor(out=tile, in0=tile, in1=ident[:], op=ALU.add).then_inc(eye_added, 1)
                elif e[0] == "normalise":
                    g = e[1]
                    pool.wait_ge(var_ready, g + 1)
                    if g >= 1:
                        pool.wait_ge(h_ready, g)
                    nc.gpsimd.tensor_tensor(out=rstd[:], in0=variance[:], in1=minus_half[:],
                                            op=ALU.pow).then_inc(rstd_ready, 1)
                    pool.wait_ge(rstd_ready, g + 1)
                    nc.gpsimd.tensor_tensor(out=shift[:], in0=minus_mean[:], in1=rstd[:],
                                            op=ALU.mult).then_inc(shift_ready, 1)
                elif e[0] == "scale":
                    g = e[1]
                    pool.wait_ge(degree_ready, g + 1)
                    nc.gpsimd.tensor_tensor(out=factor[:, g, :], in0=degree[:, g, :], in1=minus_half[:],
                                            op=ALU.pow).then_inc(factor_ready, 1)
                    pool.wait_ge(factor_ready, g + 1)
                    pool.wait_ge(raw_ready, g + 1)
                    nc.gpsimd.tensor_tensor(out=scaled[:], in0=raw[:],
                                            in1=factor[:, g, :].unsqueeze(2).broadcast_to([P, SUB, D]),
                                            op=ALU.mult).then_inc(scaled_ready, 1)
                    pool.wait_ge(scaled_ready, g + 1)
                    nc.gpsimd.tensor_copy(Sh[:, g], scaled[:]).then_inc(sh_ready, 1)
                    pool.wait_ge(sh_ready, g + 1)
                    nc.gpsimd.tensor_tensor(out=Sl[:, g], in0=scaled[:], in1=Sh[:, g].bitcast(F32),
                                            op=ALU.subtract).then_inc(s_ready, 1)
                elif e[0] == "finish":
                    pool.wait_ge(relu_ready, fins + 1)
                    pool.wait_ge(x_out_in[fins % 2], 16 * (fins // 2 + 1))
                    nc.gpsimd.tensor_tensor(out=fin[fins % 2][:], in0=fin[fins % 2][:], in1=x_out[fins % 2][:],
                                            op=ALU.add).then_inc(fin_ready, 1)
                    fins += 1

        @block.scalar
        def _(act):
            act.wait_ge(wT_made, 1)
            nc.scalar.copy(wT[:], aux[:, 0:P]).then_inc(wT_ready, 1)
            turned_out = fins = stores = 0
            for e in timeline:
                if e[0] == "unit":
                    k = e[1]
                    act.wait_ge(transposed, k + 1)
                    if k >= NAT:
                        act.wait_ge(multiplied, k - NAT + 1)
                    nc.scalar.copy(Ah[k % NAT][:], pt[k % NPT][:]).then_inc(high_ready, 1)
                elif e[0] == "sum" and sums_on_act(*e[1:]):
                    n, s = e[1:]
                    i, j = plan.loads[n][:2]
                    block_there(act, n)
                    if i == j:
                        act.wait_ge(eye_added, SUB * i + s + 1)
                    no = act_sum_no[n, s]
                    if no > 2:
                        act.wait_ge(act_summed, no - 2)
                    nc.scalar.activation(junk[:, no % 2, :], A[plan.slots[n]][:, s, :], ACT.Copy,
                                         accum_out=partial[:, i, s, j:j + 1]).then_inc(act_summed, 1)
                elif e[0] == "hidden":
                    g = e[1]
                    act.wait_ge(shift_ready, g + 1)
                    for s in range(SUB):
                        last = nc.scalar.activation(h[:, s, :], xg[:, s, :], ACT.Relu, bias=shift[:, s:s + 1],
                                                    scale=rstd[:, s:s + 1])
                    last.then_inc(h_ready, 1)
                elif e[0] == "turned":
                    g = e[1]
                    act.wait_ge(h_turned, g + 1)
                    nc.scalar.copy(hT[:], aux[:]).then_inc(hT_ready, 1)
                elif e[0] == "raw":
                    g = e[1]
                    act.wait_ge(projected, g + 1)
                    if g >= 1:
                        act.wait_ge(scaled_ready, g)
                    nc.scalar.copy(raw[:], aux[:]).then_inc(raw_ready, 1)
                elif e[0] == "turn out":
                    if turned_out == 0:
                        act.wait_ge(s_ready, G)
                    if turned_out >= 2:
                        act.wait_ge(fin_ready, turned_out - 1)
                    act.dma_start(x_out[turned_out % 2][:], x_v[e[1]]).then_inc(x_out_in[turned_out % 2], 16)
                    turned_out += 1
                elif e[0] == "finish":
                    i = e[1]
                    act.wait_ge(out_turned, fins + 1)
                    if fins >= 2:
                        act.wait_ge(stored[fins % 2], 16 * (fins // 2))
                    for s in range(SUB):
                        last = nc.scalar.activation(fin[fins % 2][:, s, :], aux[:, s * D:(s + 1) * D], ACT.Relu,
                                                    scale=factor[:, i, s:s + 1])
                    last.then_inc(relu_ready, 1)
                    fins += 1
                elif e[0] == "store":
                    act.wait_ge(fin_ready, stores + 1)
                    act.dma_start(out_v[e[1]], fin[stores % 2][:]).then_inc(stored[stores % 2], 16)
                    stores += 1
            act.wait_ge(stored[0], 16 * (G // 2))
            act.wait_ge(stored[1], 16 * (G // 2))

        @block.vector
        def _(dve):
            fins = 0
            for e in timeline:
                if e[0] == "unit":
                    k = e[1]
                    dve.wait_ge(high_ready, k + 1)
                    nc.vector.tensor_tensor(out=Al[k % NAT][:], in0=pt[k % NPT][:], in1=Ah[k % NAT][:].bitcast(F32),
                                            op=ALU.subtract).then_inc(low_ready, 1)
                elif e[0] == "sum" and not sums_on_act(*e[1:]):
                    n, s = e[1:]
                    i, j = plan.loads[n][:2]
                    block_there(dve, n)
                    if i == j:
                        dve.wait_ge(eye_added, SUB * i + s + 1)
                    nc.vector.tensor_reduce(partial[:, i, s, j:j + 1], A[plan.slots[n]][:, s, :], AXX,
                                            ALU.add).then_inc(dve_summed, 1)
                elif e[0] == "normalise":
                    g = e[1]
                    dve.wait_ge(x_in, 16 * (g + 1))
                    if g >= 1:
                        dve.wait_ge(h_ready, g)
                    for s in range(SUB):
                        last = nc.vector.bn_stats(stats[:, s, :], xg[:, s, :])
                    last.then_inc(stats_ready, 1)
                    dve.wait_ge(stats_ready, g + 1)
                    for s in range(SUB):
                        last = nc.vector.bn_aggr(moments[:, s, :], stats[:, s, :])
                    last.then_inc(moments_ready, 1)
                    dve.wait_ge(moments_ready, g + 1)
                    nc.vector.tensor_scalar(minus_mean[:], moments[:, :, 0], -1.0, None, ALU.mult)
                    nc.vector.tensor_scalar(variance[:], moments[:, :, 1], EPS, None, ALU.add).then_inc(var_ready, 1)
                elif e[0] == "scale":
                    g = e[1]
                    lasts = [n for n in range(len(plan.loads)) if group_of[n] == g and plan.loads[n][2]]
                    dve.wait_ge(act_summed, max(act_sums_by[n] for n in lasts))
                    dve.wait_ge(dve_summed, max(dve_sums_by[n] for n in lasts))
                    nc.vector.tensor_reduce(degree[:, g, :], partial[:, g, :, :], AXX, ALU.add).then_inc(degree_ready, 1)
                elif e[0] == "park":
                    i = e[1]
                    dve.wait_ge(multiplied, row_end[i, True] + 1)
                    nc.vector.tensor_copy(parked[:, i, :], acc[i % NACC][:]).then_inc(parked_ready, 1)
                elif e[0] == "gather":
                    i = e[1]
                    if fins >= 1:
                        dve.wait_ge(out_turned, fins)
                    if i < rereads:
                        dve.wait_ge(multiplied, row_end[i, False] + 1)
                        nc.vector.tensor_tensor(out=total[:], in0=acc[i % NACC][:], in1=parked[:, i, :],
                                                op=ALU.add).then_inc(total_ready, 1)
                    else:
                        dve.wait_ge(parked_ready, parks.index(i) + 1)
                        nc.vector.tensor_copy(total[:], parked[:, i, :]).then_inc(total_ready, 1)
                    fins += 1

        @block.tensor
        def _(pe):
            def turn_unit(k):
                n, i, j, t = units[k]
                if t == 0:
                    block_there(pe, n)
                    if i == j:
                        pe.wait_ge(eye_added, SUB * (i + 1))
                if k >= NPT:
                    pe.wait_ge(low_ready, k - NPT + 1)
                for s in range(SUB):
                    last = nc.tensor.transpose(pt[k % NPT][:, s * P:(s + 1) * P],
                                               A[plan.slots[n]][:, s, t * P:(t + 1) * P], ident[:])
                last.then_inc(transposed, 1)

            pe.wait_ge(w_in, 16)
            pe.wait_ge(ident_ready, 1)
            nc.tensor.transpose(aux[:, 0:P], w_rows[:], ident[:]).then_inc(wT_made, 1)
            fins = 0
            turned = 0
            for e in timeline:
                if e[0] == "unit":
                    k = e[1]
                    n, i, j, t = units[k]
                    while turned < min(k + AHEAD + 1, len(units)):
                        turn_unit(turned)
                        turned += 1
                    if k in opened and opened[k]:
                        if opened[k] <= G:
                            pe.wait_ge(parked_ready, opened[k])
                        else:
                            pe.wait_ge(total_ready, gather_no(opened[k] - G))
                    if t == 0:
                        pe.wait_ge(s_ready, j + 1)
                    pe.wait_ge(low_ready, k + 1)
                    bank = acc[i % NACC]
                    a, b = Ah[k % NAT], Al[k % NAT]
                    nc.tensor.matmul(bank[:], Sh[:, j, t, :], a[:], start=k in opened, stop=False)
                    nc.tensor.matmul(bank[:], Sh[:, j, t, :], b[:], start=False, stop=False)
                    nc.tensor.matmul(bank[:], Sl[:, j, t, :], a[:], start=False,
                                     stop=k in bank_last).then_inc(multiplied, 1)
                elif e[0] == "turn":
                    g = e[1]
                    pe.wait_ge(h_ready, g + 1)
                    pe.wait_ge(wT_ready, 1)
                    if g >= 1:
                        pe.wait_ge(raw_ready, g)
                    for s in range(SUB):
                        last = nc.tensor.transpose(aux[:, s * P:(s + 1) * P], h[:, s, :], ident[:])
                    last.then_inc(h_turned, 1)
                elif e[0] == "project":
                    g = e[1]
                    pe.wait_ge(hT_ready, g + 1)
                    for s in range(SUB):
                        last = nc.tensor.matmul(aux[:, s * D:(s + 1) * D], hT[:, s * P:(s + 1) * P], wT[:],
                                                start=True, stop=True)
                    last.then_inc(projected, 1)
                elif e[0] == "turn out":
                    pe.wait_ge(total_ready, fins + 1)
                    if fins == 0:
                        pe.wait_ge(raw_ready, G)
                    else:
                        pe.wait_ge(relu_ready, fins)
                    for s in range(SUB):
                        last = nc.tensor.transpose(aux[:, s * P:(s + 1) * P], total[:, s * P:(s + 1) * P], ident[:])
                    last.then_inc(out_turned, 1)
                    fins += 1


def kernel(x, adj, L0_gnn_W):
    import numpy as np
    import concourse.bacc as bacc
    from concourse.bass_utils import run_bass_kernel_spmd

    nc = bacc.Bacc("TRN2", target_bir_lowering=False, num_devices=1, dynamic_dma_scratch_size=1024)
    arrays = {"x": np.ascontiguousarray(x), "adj": np.ascontiguousarray(adj), "w": np.ascontiguousarray(L0_gnn_W)}
    aps = [nc.dram_tensor(n, a.shape, mybir.dt.from_np(a.dtype), kind="ExternalInput").ap() for n, a in arrays.items()]
    out = nc.dram_tensor("out", arrays["x"].shape, F32, kind="ExternalOutput").ap()
    gcn_kernel(nc, *aps, out)
    return run_bass_kernel_spmd(nc, [arrays], core_ids=[0]).results[0]["out"]
```

```python
import concourse.bass as bass
from concourse import mybir
from contextlib import ExitStack

F32 = mybir.dt.float32
ALU = mybir.AluOpType
ACT = mybir.ActivationFunctionType
AXX = mybir.AxisListType.X

P = 128
Q = 32
NQ = P // Q
SUB = 4
B = P * SUB
M = B // Q
BAND = 3
LEAD = 1
FIRST = 2
SLOTS = 16
NAT = 5
FETCH_LAG = 12
DEGREE_LAG = 0.75
PARK_LAG = 1.5
GATHER_APART = 1.25
NACC = BAND + 3


class Plan:

    def __init__(self, groups):
        self.groups = groups
        self.loads, self.units, events = [], [], []
        at, where, arrived = 0.0, {}, []

        def event(pos, *what):
            events.append((pos, len(events), what))

        def load(i, j, summed, used):
            arrived.append(len(self.loads) + 1.0)
            self.loads.append((i, j, summed, used))
            return len(self.loads) - 1

        def products(blocks, start, span):
            nonlocal at
            n = len(blocks) * SUB
            for q in range(n):
                i, j = blocks[q // SUB]
                m = where[i, j]
                at = max(at, start + span * q / n, arrived[m])
                event(at, "unit", len(self.units))
                self.units.append((m, i, j, q % SUB))
                if q % SUB == SUB - 1:
                    if j == min(i + BAND, groups - 1):
                        event(at + PARK_LAG, "park", i)

        lead = []
        for g in range(groups):
            held = [(i, g - 1) for i in range(max(0, g - 1 - BAND), g)] if g else []
            off = held[1:][-LEAD:]
            held = lead + held[:len(held) - len(off)]
            lead = off
            left = [(g, j) for j in range(g)]
            far = [(g, j) for j in range(g + BAND + 1, groups)]
            near = [(g, j) for j in range(min(g + BAND, groups - 1), g - 1, -1)]
            key = {b: (len(held) + m - 1) / (len(held) + len(left)) for m, b in enumerate(left)}
            key |= {b: (m + 0.5) / len(far) for m, b in enumerate(far)}
            for b in sorted(key, key=key.get) + near:
                where[b] = load(*b, True, b not in far)
                for s in range(SUB):
                    event(arrived[-1] + s / SUB, "sum", where[b], s)
            start = g * groups + 1.0
            for k, what in enumerate(("normalise", "hidden", "turn", "turned", "project", "raw")):
                event(start + 3 + k, what, g)
            products(held + left, start + 0.1, groups - 0.2)
            event((g + 1) * groups + 1.0, "fold", g)
            event((g + 1) * groups + 1.0 + DEGREE_LAG, "scale", g)
        g = groups
        products(lead, g * groups + 1.1, len(lead))
        done = []
        for i in [0] + list(range(groups - BAND - 2, 0, -1)):
            blocks = [(i, j) for j in range(i + BAND + 1, groups)]
            for b in blocks:
                where[b] = load(*b, False, True)
            if i == 0:
                products(blocks[:FIRST], at, FIRST)
                last = [(k, g - 1) for k in range(max(0, g - 1 - BAND), g)]
                products(last, at, len(last))
                done += [(at + 4, k) for k, _ in last]
                blocks = blocks[FIRST:]
            products(blocks, at, len(blocks))
            done.append((at + PARK_LAG, i))
        pos = 0
        for ready, i in sorted(done):
            pos = max(pos + GATHER_APART, ready)
            event(pos, "gather", i)
            event(pos + 1, "turn out", i)
            event(pos + 1.75, "finish", i)
            event(pos + 4, "store", i)
        self.timeline = [what for _, _, what in sorted(events)]

        last_use, first = {}, {}
        for pos, e in enumerate(self.timeline):
            m = e[1] if e[0] == "sum" else self.units[e[1]][0] if e[0] == "unit" else None
            if m is not None:
                last_use[m] = pos
        holds = [None] * SLOTS
        self.slots, self.evicted = [], []
        for n in range(len(self.loads)):
            s = min(range(SLOTS), key=lambda s: (-1, s) if holds[s] is None else (last_use[holds[s]], s))
            self.slots.append(s)
            self.evicted.append(holds[s])
            holds[s] = n
        after = {}
        for n, m in enumerate(self.evicted):
            at = -1 if m is None else min(last_use[m] + FETCH_LAG, len(self.timeline) - 1)
            after.setdefault(max([at] + [k for k in after]), []).append(n)
        merged = [("fetch", n) for n in after.get(-1, [])]
        for pos, e in enumerate(self.timeline):
            merged += [e] + [("fetch", n) for n in after.get(pos, [])]
        self.timeline = merged


def sums_on_act(far, i, n, s):
    if far:
        return True
    share = min(0.8 + 3 * max(i - 2, 0) / 16, 2.5)
    return s >= SUB - (int(share * (n + 1)) - int(share * n))



def gcn_kernel(nc, x, adj, w, out):
    N, D = x.shape
    G = N // B
    EPS = 1e-5
    plan = Plan(G)
    units, timeline = plan.units, plan.timeline

    x_v = x.rearrange("(g q t c) d -> g q c t d", q=NQ, t=SUB, c=Q)
    out_v = out.rearrange("(g q t c) d -> g q c t d", q=NQ, t=SUB, c=Q)
    block_v = adj.rearrange("(i m r) (j q c) -> i j q r m c", m=M, r=Q, q=NQ, c=P)
    far_v = adj.rearrange("(i q t r) (j c) -> i j q r t c", q=NQ, t=SUB, r=Q, c=B)
    assert Q * SUB == P and plan.groups * B == N

    ctx = ExitStack()
    with ctx:
        def sb(name, shape, dt=F32):
            return ctx.enter_context(nc.sbuf_tensor(name, shape, dt))

        def pb(name):
            return ctx.enter_context(nc.psum_tensor(name, [P, B], F32))

        def sem(name):
            return ctx.enter_context(nc.semaphore(name))

        A = [sb(f"A{r}", [P, M * P]) for r in range(SLOTS)]
        AT = [sb(f"AT{r}", [P, B]) for r in range(NAT)]
        S = sb("S", [P, G, SUB, D])
        parked = sb("parked", [P, G, B])
        near_sums = sb("near_sums", [P, 2, G, M])
        far_sums = sb("far_sums", [P, 2, SUB, G])
        near_sum = sb("near_sum", [P, M])
        far_sum = sb("far_sum", [P, SUB])
        same_row = sb("same_row", [P, Q])
        degree = sb("degree", [P, G, SUB])
        factor = sb("factor", [P, G, SUB])
        minus_half = sb("minus_half", [P, SUB])
        ident = sb("ident", [P, P])
        w_rows = sb("w_rows", [P, D])
        wT = sb("wT", [P, P])
        xg = sb("xg", [P, SUB, D])
        h = sb("h", [P, SUB, D])
        hT = sb("hT", [P, B])
        raw = sb("raw", [P, SUB, D])
        spare = sb("spare", [P, SUB, D])
        stats = sb("stats", [P, SUB, 6])
        moments = sb("moments", [P, SUB, 2])
        variance = sb("variance", [P, SUB])
        minus_mean = sb("minus_mean", [P, SUB])
        rstd = sb("rstd", [P, SUB])
        shift = sb("shift", [P, SUB])
        junk = sb("junk", [P, 2, B], mybir.dt.bfloat16)
        total, fin, x_out = hT, (spare, h), (xg, raw)

        acc = [pb(f"acc{r}") for r in range(NACC)]
        aux = pb("aux")
        fold = pb("fold")

        block_in = [sem(f"block_in{r}") for r in range(SLOTS)]
        w_in = sem("w_in")
        x_in = sem("x_in")
        x_out_in = [sem(f"x_out_in{r}") for r in range(2)]
        stored = [sem(f"stored{r}") for r in range(2)]
        ident_ready = sem("ident_ready")
        consts_ready = sem("consts_ready")
        wT_made = sem("wT_made")
        wT_ready = sem("wT_ready")
        eye_added = sem("eye_added")
        unit_ready = sem("unit_ready")
        multiplied = sem("multiplied")
        act_summed = sem("act_summed")
        dve_summed = sem("dve_summed")
        parked_ready = sem("parked_ready")
        stats_ready = sem("stats_ready")
        moments_ready = sem("moments_ready")
        var_ready = sem("var_ready")
        rstd_ready = sem("rstd_ready")
        shift_ready = sem("shift_ready")
        h_ready = sem("h_ready")
        h_turned = sem("h_turned")
        hT_ready = sem("hT_ready")
        projected = sem("projected")
        raw_ready = sem("raw_ready")
        same_row_ready = sem("same_row_ready")
        near_sum_ready = sem("near_sum_ready")
        folded = sem("folded")
        degree_ready = sem("degree_ready")
        factor_ready = sem("factor_ready")
        s_ready = sem("s_ready")
        total_ready = sem("total_ready")
        out_turned = sem("out_turned")
        relu_ready = sem("relu_ready")
        fin_ready = sem("fin_ready")

        group_of = [i for i, _, _, _ in plan.loads]

        def far(n):
            return not plan.loads[n][3]

        def on_act(n, s):
            return sums_on_act(far(n), group_of[n], n, s)

        act_sum_no, dve_sum_no = {}, {}
        for e in timeline:
            if e[0] == "sum":
                to = act_sum_no if on_act(*e[1:]) else dve_sum_no
                to[e[1:]] = len(to) + 1
        act_sums_by, dve_sums_by, diagonal_by = {}, {}, {}
        for (n, s), k in act_sum_no.items():
            act_sums_by[n] = k
        for (n, s), k in dve_sum_no.items():
            dve_sums_by[n] = k
        last_unit = {}
        for k, (n, i, j, t) in enumerate(units):
            last_unit[n] = k
        uses = []
        for n in range(len(plan.loads)):
            m = plan.evicted[n]
            uses.append(1 if m is None else uses[m] + 1)
        parks = [e[1] for e in timeline if e[0] == "park"]
        gathers = [e[1] for e in timeline if e[0] == "gather"]
        rereads = G - BAND - 1

        bank = {}
        starts = {}
        row_end = {}
        emptied_by = {}
        free = [(b, None) for b in range(NACC)]
        for e in timeline:
            if e[0] == "unit":
                k = e[1]
                row = units[k][1], plan.loads[units[k][0]][2]
                if row not in bank:
                    starts[row] = k
                    bank[row], emptied_by[row] = free.pop(0)
                row_end[row] = k
            elif e[0] == "park" or (e[0] == "gather" and e[1] < rereads):
                free.append((bank[e[1], e[0] == "park"], e))

        def block_there(eng, n):
            eng.wait_ge(block_in[plan.slots[n]], 16 * NQ * uses[n])

        def block_free(eng, n):
            m = plan.evicted[n]
            if m is None:
                return
            if m in act_sums_by:
                eng.wait_ge(act_summed, act_sums_by[m])
            if m in dve_sums_by:
                eng.wait_ge(dve_summed, dve_sums_by[m])
            if m in last_unit:
                eng.wait_ge(unit_ready, last_unit[m] + 1)

        def load_quadrants(eng, n, quadrants):
            i, j = plan.loads[n][:2]
            for q in quadrants:
                to = A[plan.slots[n]][Q * q:Q * (q + 1), :]
                if far(n):
                    to, of = to.rearrange("r (t c) -> r t c", t=SUB), far_v[i, j, q]
                else:
                    to, of = to.rearrange("r (m c) -> r m c", m=M), block_v[i, j, q]
                eng.dma_start(to, of).then_inc(block_in[plan.slots[n]], 16)

        def by_node(rows):
            return rows.rearrange("f (q t c) -> f q t c", q=NQ, t=SUB)

        def nodes_in(eng, to, g, signal):
            for q in range(NQ):
                eng.dma_start(to[Q * q:Q * (q + 1)], x_v[g, q]).then_inc(signal, 16)

        block = ctx.enter_context(nc.Block())

        @block.sync
        def _(sp):
            sp.dma_start(w_rows[:], w[:, :]).then_inc(w_in, 16)
            nodes_in(sp, xg, 0, x_in)
            for n, (i, j, summed, used) in enumerate(plan.loads):
                if summed and n % G == G // 2 and n // G + 1 < G:
                    g = n // G + 1
                    sp.wait_ge(h_ready, g)
                    nodes_in(sp, xg, g, x_in)
                block_free(sp, n)
                load_quadrants(sp, n, (0, 1))

        @block.gpsimd
        def _(pool):
            nc.gpsimd.memset(ident[:], 0.0).then_inc(consts_ready, 1)
            pool.wait_ge(consts_ready, 1)
            nc.gpsimd.affine_select(out=ident[:], in_=ident[:], compare_op=ALU.not_equal, fill=1.0, base=0,
                                    pattern=[[-1, P]], channel_multiplier=1).then_inc(ident_ready, 1)
            nc.gpsimd.memset(minus_half[:], -0.5).then_inc(consts_ready, 1)
            pool.wait_ge(ident_ready, 1)
            pool.wait_ge(consts_ready, 2)
            eyes, fins = 0, 0
            for e in timeline:
                if e[0] == "sum" and plan.loads[e[1]][0] == plan.loads[e[1]][1]:
                    n, t = e[1:]
                    block_there(pool, n)
                    tile = A[plan.slots[n]][:].rearrange("p (q t c) -> p q t c", q=NQ, t=SUB)[
                        :, :, t, Q * t:Q * (t + 1)]
                    nc.gpsimd.tensor_tensor(out=tile, in0=tile, in1=ident[:].rearrange("p (q c) -> p q c", q=NQ),
                                            op=ALU.add).then_inc(eye_added, 1)
                elif e[0] == "normalise":
                    g = e[1]
                    pool.wait_ge(var_ready, g + 1)
                    if g >= 1:
                        pool.wait_ge(h_ready, g)
                    nc.gpsimd.tensor_tensor(out=rstd[:], in0=variance[:], in1=minus_half[:],
                                            op=ALU.pow).then_inc(rstd_ready, 1)
                    pool.wait_ge(rstd_ready, g + 1)
                    nc.gpsimd.tensor_tensor(out=shift[:], in0=minus_mean[:], in1=rstd[:],
                                            op=ALU.mult).then_inc(shift_ready, 1)
                elif e[0] == "scale":
                    g = e[1]
                    pool.wait_ge(degree_ready, g + 1)
                    nc.gpsimd.tensor_tensor(out=factor[:, g, :], in0=degree[:, g, :], in1=minus_half[:],
                                            op=ALU.pow).then_inc(factor_ready, 1)
                    pool.wait_ge(factor_ready, g + 1)
                    pool.wait_ge(raw_ready, g + 1)
                    nc.gpsimd.tensor_tensor(out=S[:, g], in0=raw[:],
                                            in1=factor[:, g, :].unsqueeze(2).broadcast_to([P, SUB, D]),
                                            op=ALU.mult).then_inc(s_ready, 1)
                elif e[0] == "finish":
                    pool.wait_ge(relu_ready, fins + 1)
                    pool.wait_ge(x_out_in[fins % 2], 16 * NQ * (fins // 2 + 1))
                    nc.gpsimd.tensor_tensor(out=fin[fins % 2][:], in0=fin[fins % 2][:], in1=x_out[fins % 2][:],
                                            op=ALU.add).then_inc(fin_ready, 1)
                    fins += 1

        @block.scalar
        def _(act):
            act.wait_ge(wT_made, 1)
            nc.scalar.copy(wT[:], aux[:, 0:P]).then_inc(wT_ready, 1)
            turned_out = fins = stores = 0
            for e in timeline:
                if e[0] == "fetch":
                    block_free(act, e[1])
                    load_quadrants(act, e[1], (2, 3))
                elif e[0] == "sum" and on_act(*e[1:]):
                    n, s = e[1:]
                    i, j = plan.loads[n][:2]
                    block_there(act, n)
                    if i == j:
                        act.wait_ge(eye_added, SUB * (i + 1))
                    if i >= 2:
                        act.wait_ge(degree_ready, i - 1)
                    no = act_sum_no[n, s]
                    if no > 2:
                        act.wait_ge(act_summed, no - 2)
                    if far(n):
                        nc.scalar.activation(junk[:, no % 2, :], A[plan.slots[n]][:, s * B:(s + 1) * B], ACT.Copy,
                                             accum_out=far_sums[:, i % 2, s, j:j + 1]).then_inc(act_summed, 1)
                    else:
                        for m in range(SUB * s, SUB * (s + 1)):
                            last = nc.scalar.activation(
                                junk[:, no % 2, m % SUB * P:(m % SUB + 1) * P],
                                A[plan.slots[n]][:, m * P:(m + 1) * P], ACT.Copy,
                                accum_out=near_sums[:, i % 2, j, m:m + 1])
                        last.then_inc(act_summed, 1)
                elif e[0] == "park":
                    i = e[1]
                    act.wait_ge(multiplied, row_end[i, True] + 1)
                    nc.scalar.copy(parked[:, i, :], acc[bank[i, True]][:]).then_inc(parked_ready, 1)
                elif e[0] == "hidden":
                    g = e[1]
                    act.wait_ge(shift_ready, g + 1)
                    for s in range(SUB):
                        last = nc.scalar.activation(h[:, s, :], xg[:, s, :], ACT.Relu, bias=shift[:, s:s + 1],
                                                    scale=rstd[:, s:s + 1])
                    last.then_inc(h_ready, 1)
                elif e[0] == "turned":
                    g = e[1]
                    act.wait_ge(h_turned, g + 1)
                    nc.scalar.copy(hT[:], aux[:]).then_inc(hT_ready, 1)
                elif e[0] == "raw":
                    g = e[1]
                    act.wait_ge(projected, g + 1)
                    if g >= 1:
                        act.wait_ge(s_ready, g)
                    nc.scalar.copy(raw[:], aux[:]).then_inc(raw_ready, 1)
                elif e[0] == "turn out":
                    if turned_out == 0:
                        act.wait_ge(s_ready, G)
                    if turned_out >= 2:
                        act.wait_ge(fin_ready, turned_out - 1)
                    nodes_in(act, x_out[turned_out % 2], e[1], x_out_in[turned_out % 2])
                    turned_out += 1
                elif e[0] == "finish":
                    i = e[1]
                    act.wait_ge(out_turned, fins + 1)
                    if fins >= 2:
                        act.wait_ge(stored[fins % 2], 16 * NQ * (fins // 2))
                    for s in range(SUB):
                        last = nc.scalar.activation(fin[fins % 2][:, s, :], aux[:, s * D:(s + 1) * D], ACT.Relu,
                                                    scale=factor[:, i, s:s + 1])
                    last.then_inc(relu_ready, 1)
                    fins += 1
                elif e[0] == "store":
                    act.wait_ge(fin_ready, stores + 1)
                    for q in range(NQ):
                        act.dma_start(out_v[e[1], q], fin[stores % 2][Q * q:Q * (q + 1)]).then_inc(
                            stored[stores % 2], 16)
                    stores += 1
            act.wait_ge(stored[0], 16 * NQ * (G // 2))
            act.wait_ge(stored[1], 16 * NQ * (G // 2))

        @block.vector
        def _(dve):
            dve.wait_ge(ident_ready, 1)
            nc.vector.tensor_reduce(same_row[:], ident[:].rearrange("p (q c) -> p c q", q=NQ), AXX,
                                    ALU.add).then_inc(same_row_ready, 1)
            fins = 0
            for e in timeline:
                if e[0] == "unit":
                    k = e[1]
                    n, i, j, t = units[k]
                    block_there(dve, n)
                    if i == j:
                        dve.wait_ge(eye_added, SUB * (i + 1))
                    if k >= NAT:
                        dve.wait_ge(multiplied, k - NAT + 1)
                    nc.vector.transpose(AT[k % NAT][:].rearrange("p (m r) -> p m r", m=M),
                                        A[plan.slots[n]][:].rearrange("p (m c) -> p m c", m=M)[
                                            :, :, Q * t:Q * (t + 1)]).then_inc(unit_ready, 1)
                elif e[0] == "sum" and not on_act(*e[1:]):
                    n, s = e[1:]
                    i, j = plan.loads[n][:2]
                    block_there(dve, n)
                    if i == j:
                        dve.wait_ge(eye_added, SUB * (i + 1))
                    nc.vector.tensor_reduce(near_sums[:, i % 2, j, SUB * s:SUB * (s + 1)],
                                            A[plan.slots[n]][:, s * B:(s + 1) * B].rearrange(
                                                "p (m c) -> p m c", m=SUB),
                                            AXX, ALU.add).then_inc(dve_summed, 1)
                elif e[0] == "normalise":
                    g = e[1]
                    dve.wait_ge(x_in, 16 * NQ * (g + 1))
                    if g >= 1:
                        dve.wait_ge(h_ready, g)
                    for s in range(SUB):
                        last = nc.vector.bn_stats(stats[:, s, :], xg[:, s, :])
                    last.then_inc(stats_ready, 1)
                    dve.wait_ge(stats_ready, g + 1)
                    for s in range(SUB):
                        last = nc.vector.bn_aggr(moments[:, s, :], stats[:, s, :])
                    last.then_inc(moments_ready, 1)
                    dve.wait_ge(moments_ready, g + 1)
                    nc.vector.tensor_scalar(minus_mean[:], moments[:, :, 0], -1.0, None, ALU.mult)
                    nc.vector.tensor_scalar(variance[:], moments[:, :, 1], EPS, None, ALU.add).then_inc(var_ready, 1)
                elif e[0] == "fold":
                    g = e[1]
                    lasts = [n for n in range(len(plan.loads)) if group_of[n] == g and plan.loads[n][2]]
                    dve.wait_ge(act_summed, max(act_sums_by.get(n, 0) for n in lasts))
                    dve.wait_ge(dve_summed, max(dve_sums_by.get(n, 0) for n in lasts))
                    if g >= 1:
                        dve.wait_ge(folded, g)
                    ends = min(g + BAND + 1, G)
                    if ends < G:
                        nc.vector.tensor_reduce(far_sum[:], far_sums[:, g % 2, :, ends:G], AXX, ALU.add)
                    nc.vector.tensor_reduce(near_sum[:], near_sums[:, g % 2, 0:ends, :].rearrange("p j m -> p m j"),
                                            AXX, ALU.add).then_inc(near_sum_ready, 1)
                elif e[0] == "scale":
                    g = e[1]
                    dve.wait_ge(folded, g + 1)
                    if g + BAND + 1 < G:
                        nc.vector.tensor_tensor(out=degree[:, g, :], in0=fold[:, 0:SUB], in1=far_sum[:],
                                                op=ALU.add).then_inc(degree_ready, 1)
                    else:
                        nc.vector.tensor_copy(degree[:, g, :], fold[:, 0:SUB]).then_inc(degree_ready, 1)
                elif e[0] == "gather":
                    i = e[1]
                    nodes = total[:].rearrange("f (t q c) -> f q t c", q=NQ, t=SUB)
                    if fins >= 1:
                        dve.wait_ge(out_turned, fins)
                    if i < rereads:
                        dve.wait_ge(multiplied, row_end[i, False] + 1)
                        nc.vector.tensor_tensor(out=nodes, in0=by_node(acc[bank[i, False]][:]), in1=by_node(parked[:, i, :]),
                                                op=ALU.add).then_inc(total_ready, 1)
                    else:
                        dve.wait_ge(parked_ready, parks.index(i) + 1)
                        nc.vector.tensor_copy(nodes, by_node(parked[:, i, :])).then_inc(total_ready, 1)
                    fins += 1

        @block.tensor
        def _(pe):
            pe.wait_ge(w_in, 16)
            pe.wait_ge(ident_ready, 1)
            nc.tensor.transpose(aux[:, 0:P], w_rows[:], ident[:]).then_inc(wT_made, 1)
            fins = 0
            for e in timeline:
                if e[0] == "unit":
                    k = e[1]
                    n, i, j, t = units[k]
                    row = i, plan.loads[n][2]
                    if k == starts[row] and emptied_by[row]:
                        what, former = emptied_by[row]
                        if what == "park":
                            pe.wait_ge(parked_ready, parks.index(former) + 1)
                        else:
                            pe.wait_ge(total_ready, gathers.index(former) + 1)
                    if t == 0:
                        pe.wait_ge(s_ready, j + 1)
                    pe.wait_ge(unit_ready, k + 1)
                    nc.tensor.matmul(acc[bank[row]][:], S[:, j, t, :], AT[k % NAT][:], start=k == starts[row],
                                     stop=k == row_end[row]).then_inc(multiplied, 1)
                elif e[0] == "turn":
                    g = e[1]
                    pe.wait_ge(h_ready, g + 1)
                    pe.wait_ge(wT_ready, 1)
                    if g >= 1:
                        pe.wait_ge(raw_ready, g)
                    for s in range(SUB):
                        last = nc.tensor.transpose(aux[:, s * P:(s + 1) * P], h[:, s, :], ident[:])
                    last.then_inc(h_turned, 1)
                elif e[0] == "project":
                    g = e[1]
                    pe.wait_ge(hT_ready, g + 1)
                    for s in range(SUB):
                        last = nc.tensor.matmul(aux[:, s * D:(s + 1) * D], hT[:, s * P:(s + 1) * P], wT[:],
                                                start=True, stop=True)
                    last.then_inc(projected, 1)
                elif e[0] == "fold":
                    g = e[1]
                    pe.wait_ge(near_sum_ready, g + 1)
                    pe.wait_ge(same_row_ready, 1)
                    for q in range(NQ):
                        last = nc.tensor.matmul(fold[Q * q:Q * (q + 1), 0:SUB], same_row[:],
                                                near_sum[:, SUB * q:SUB * (q + 1)], start=True, stop=True)
                    last.then_inc(folded, 1)
                elif e[0] == "turn out":
                    pe.wait_ge(total_ready, fins + 1)
                    if fins == 0:
                        pe.wait_ge(raw_ready, G)
                    else:
                        pe.wait_ge(relu_ready, fins)
                    for s in range(SUB):
                        last = nc.tensor.transpose(
                            aux[:, s * P:(s + 1) * P],
                            total[:, s * P:(s + 1) * P], ident[:])
                    last.then_inc(out_turned, 1)
                    fins += 1


def kernel(x, adj, L0_gnn_W):
    import numpy as np
    import concourse.bacc as bacc
    from concourse.bass_utils import run_bass_kernel_spmd

    nc = bacc.Bacc("TRN2", target_bir_lowering=False, num_devices=1, dynamic_dma_scratch_size=1024)
    arrays = {"x": np.ascontiguousarray(x), "adj": np.ascontiguousarray(adj), "w": np.ascontiguousarray(L0_gnn_W)}
    aps = [nc.dram_tensor(n, a.shape, mybir.dt.from_np(a.dtype), kind="ExternalInput").ap() for n, a in arrays.items()]
    out = nc.dram_tensor("out", arrays["x"].shape, F32, kind="ExternalOutput").ap()
    gcn_kernel(nc, *aps, out)
    return run_bass_kernel_spmd(nc, [arrays], core_ids=[0]).results[0]["out"]
```

```python
import concourse.bass as bass
from concourse import mybir
from contextlib import ExitStack

F32 = mybir.dt.float32
ALU = mybir.AluOpType
ACT = mybir.ActivationFunctionType
AXX = mybir.AxisListType.X

P = 128
Q = 32
NQ = P // Q
SUB = 4
B = P * SUB
M = B // Q
BAND = 3
WIDER = 3
LEAD = 1
FIRST = 2
SLOTS = 17
PAIR = 2
NAT = 3
NACC = BAND + 3
FETCH_LAG = 9

DEGREE_LAG = 0.75
PARK_LAG = 1.5
GATHER_APART = 2


def last_held(i, groups):
    return min(i + BAND + (i % WIDER == 0), groups - 1)


class Plan:

    def __init__(self, groups):
        self.groups = groups
        self.loads, self.units, events = [], [], []
        at, where, arrived = 0.0, {}, []

        def event(pos, *what):
            events.append((pos, len(events), what))

        def load(i, j, summed, used):
            arrived.append(len(self.loads) + 1.0)
            self.loads.append((i, j, summed, used))
            return len(self.loads) - 1

        def products(blocks, start, span):
            nonlocal at
            n = len(blocks) * SUB
            for q in range(n):
                i, j = blocks[q // SUB]
                m = where[i, j]
                summed = self.loads[m][2]
                at = max(at, start + span * q / n, arrived[m])
                event(at, "unit", len(self.units))
                self.units.append((m, i, j, q % SUB))
                if q % SUB == SUB - 1:
                    if summed and j == last_held(i, groups):
                        if j < groups - 1:
                            event(at + PARK_LAG, "park", i)
                        else:
                            done.append((at + PARK_LAG, i))

        done = []
        lead = []
        for g in range(groups):
            held = [(i, g - 1) for i in range(g) if g - 1 <= last_held(i, groups)]
            off = held[1:][-LEAD:]
            held = lead + held[:len(held) - len(off)]
            lead = off
            left = [(g, j) for j in range(g)]
            far = [(g, j) for j in range(last_held(g, groups) + 1, groups)]
            near = [(g, j) for j in range(last_held(g, groups), g - 1, -1)]
            key = {b: (len(held) + m - 1) / (len(held) + len(left)) for m, b in enumerate(left)}
            key |= {b: (m + 0.5) / len(far) for m, b in enumerate(far)}
            for b in sorted(key, key=key.get) + near:
                where[b] = load(*b, True, b not in far)
                for s in range(SUB):
                    event(arrived[-1] + s / SUB, "sum", where[b], s)
            start = g * groups + 1.0
            event(start + 3, "normalise", g)
            event(start + 4, "hidden", g)
            products(held + left, start + 0.1, groups - 0.2)
            event((g + 1) * groups + 1.0, "fold", g)
            event((g + 1) * groups + 1.0 + DEGREE_LAG, "scale", g)
        g = groups
        products(lead, g * groups + 1.1, len(lead))
        again = [i for i in range(groups) if last_held(i, groups) < groups - 1]
        for i in again[:1] + again[:0:-1]:
            blocks = [(i, j) for j in range(last_held(i, groups) + 1, groups)]
            for b in blocks:
                where[b] = load(*b, False, True)
            if i == 0:
                products(blocks[:FIRST], at, FIRST)
                last = [(k, g - 1) for k in range(g) if k not in again]
                products(last, at, len(last))
                blocks = blocks[FIRST:]
            products(blocks, at, len(blocks))
            done.append((at + PARK_LAG, i))
        pos = 0
        for ready, i in sorted(done):
            pos = max(pos + GATHER_APART, ready)
            event(pos, "gather", i)
            event(pos + 1, "project", i)
            event(pos + 1.75, "finish", i)
            event(pos + 4, "store", i)
        self.timeline = [what for _, _, what in sorted(events)]

        last_use = {}
        for pos, e in enumerate(self.timeline):
            m = e[1] if e[0] == "sum" else self.units[e[1]][0] if e[0] == "unit" else None
            if m is not None:
                last_use[m] = pos
        holds = [None] * SLOTS
        self.slots, self.evicted = [], []
        for n in range(len(self.loads)):
            s = min(range(SLOTS), key=lambda s: (-1, s) if holds[s] is None else (last_use[holds[s]], s))
            self.slots.append(s)
            self.evicted.append(holds[s])
            holds[s] = n
        after = {}
        for n, m in enumerate(self.evicted):
            at = -1 if m is None else min(last_use[m] + FETCH_LAG, len(self.timeline) - 1)
            after.setdefault(max([at] + [k for k in after]), []).append(n)
        merged = [("fetch", n) for n in after.get(-1, [])]
        for pos, e in enumerate(self.timeline):
            merged += [e] + [("fetch", n) for n in after.get(pos, [])]
        self.timeline = merged


def sums_on_act(far, i, n, s):
    if far:
        return True
    share = min(0.8 + 3 * max(i - 2, 0) / 16, 2.5)
    return s >= SUB - (int(share * (n + 1)) - int(share * n))


def gcn_kernel(nc, x, adj, w, out):
    N, D = x.shape
    G = N // B
    EPS = 1e-5
    plan = Plan(G)
    units, timeline = plan.units, plan.timeline

    x_v = x.rearrange("(g q t c) d -> g q c t d", q=NQ, t=SUB, c=Q)
    out_v = out.rearrange("(g q t c) d -> g q c t d", q=NQ, t=SUB, c=Q)
    block_v = adj.rearrange("(i m r) (j q c) -> i j q r m c", m=M, r=Q, q=NQ, c=P)
    far_v = adj.rearrange("(i q t r) (j c) -> i j q r t c", q=NQ, t=SUB, r=Q, c=B)
    assert Q * SUB == P == D and G * B == N and SUB % PAIR == 0

    ctx = ExitStack()
    with ctx:
        def sb(name, shape, dt=F32):
            return ctx.enter_context(nc.sbuf_tensor(name, shape, dt))

        def pb(name):
            return ctx.enter_context(nc.psum_tensor(name, [P, B], F32))

        def sem(name):
            return ctx.enter_context(nc.semaphore(name))

        A = [sb(f"A{r}", [P, M * P]) for r in range(SLOTS)]
        AT = [sb(f"AT{r}", [P, PAIR, B]) for r in range(NAT)]
        S = sb("S", [P, G, SUB, D])
        parked = sb("parked", [P, max(e[1] for e in timeline if e[0] == "park") + 1, B])
        near_sums = sb("near_sums", [P, 2, G, M])
        far_sums = sb("far_sums", [P, 2, SUB, G])
        near_sum = sb("near_sum", [P, M])
        far_sum = sb("far_sum", [P, SUB])
        same_row = sb("same_row", [P, Q])
        degree = sb("degree", [P, G, SUB])
        factor = sb("factor", [P, G, SUB])
        minus_half = sb("minus_half", [P, SUB])
        ident = sb("ident", [P, P])
        w_rows = sb("w_rows", [P, D])
        wT = sb("wT", [P, P])
        xg = sb("xg", [P, SUB, D])
        total = sb("total", [P, B])
        x_out = (xg, sb("x_out", [P, SUB, D]))
        fin = [sb(f"fin{r}", [P, SUB, D]) for r in range(2)]
        stats = sb("stats", [P, SUB, 6])
        moments = sb("moments", [P, SUB, 2])
        variance = sb("variance", [P, SUB])
        minus_mean = sb("minus_mean", [P, SUB])
        rstd = sb("rstd", [P, SUB])
        shift = sb("shift", [P, SUB])
        junk = sb("junk", [P, 2, B], mybir.dt.bfloat16)

        acc = [pb(f"acc{r}") for r in range(NACC)]
        aux = pb("aux")
        fold = pb("fold")

        block_in = [sem(f"block_in{r}") for r in range(SLOTS)]
        w_in = sem("w_in")
        x_in = sem("x_in")
        x_out_in = [sem(f"x_out_in{r}") for r in range(2)]
        stored = [sem(f"stored{r}") for r in range(2)]
        ident_ready = sem("ident_ready")
        consts_ready = sem("consts_ready")
        wT_made = sem("wT_made")
        wT_ready = sem("wT_ready")
        eye_added = sem("eye_added")
        pair_ready = sem("pair_ready")
        multiplied = sem("multiplied")
        act_summed = sem("act_summed")
        dve_summed = sem("dve_summed")
        parked_ready = sem("parked_ready")
        stats_ready = sem("stats_ready")
        moments_ready = sem("moments_ready")
        var_ready = sem("var_ready")
        rstd_ready = sem("rstd_ready")
        shift_ready = sem("shift_ready")
        h_ready = sem("h_ready")
        same_row_ready = sem("same_row_ready")
        near_sum_ready = sem("near_sum_ready")
        folded = sem("folded")
        degree_ready = sem("degree_ready")
        factor_ready = sem("factor_ready")
        s_ready = sem("s_ready")
        total_ready = sem("total_ready")
        projected = sem("projected")
        relu_ready = sem("relu_ready")
        fin_ready = sem("fin_ready")

        group_of = [i for i, _, _, _ in plan.loads]

        def far(n):
            return not plan.loads[n][3]

        def on_act(n, s):
            return sums_on_act(far(n), group_of[n], n, s)

        act_sum_no, dve_sum_no = {}, {}
        for e in timeline:
            if e[0] == "sum":
                to = act_sum_no if on_act(*e[1:]) else dve_sum_no
                to[e[1:]] = len(to) + 1
        act_sums_by, dve_sums_by = {}, {}
        for (n, s), k in act_sum_no.items():
            act_sums_by[n] = k
        for (n, s), k in dve_sum_no.items():
            dve_sums_by[n] = k
        last_unit = {}
        for k, (n, i, j, t) in enumerate(units):
            last_unit[n] = k
        uses = []
        for n in range(len(plan.loads)):
            m = plan.evicted[n]
            uses.append(1 if m is None else uses[m] + 1)
        parks = [e[1] for e in timeline if e[0] == "park"]
        gathers = [e[1] for e in timeline if e[0] == "gather"]
        read_again = set(parks)

        bank = {}
        starts = {}
        row_end = {}
        emptied_by = {}
        free = [(b, None) for b in range(NACC)]
        for e in timeline:
            if e[0] == "unit":
                k = e[1]
                row = units[k][1], plan.loads[units[k][0]][2]
                if row not in bank:
                    starts[row] = k
                    bank[row], emptied_by[row] = free.pop(0)
                row_end[row] = k
            elif e[0] in ("park", "gather"):
                free.append((bank[e[1], e[0] == "park" or e[1] not in read_again], e))

        def block_there(eng, n):
            eng.wait_ge(block_in[plan.slots[n]], 16 * NQ * uses[n])

        def block_free(eng, n):
            m = plan.evicted[n]
            if m is None:
                return
            if m in act_sums_by:
                eng.wait_ge(act_summed, act_sums_by[m])
            if m in dve_sums_by:
                eng.wait_ge(dve_summed, dve_sums_by[m])
            if m in last_unit:
                eng.wait_ge(pair_ready, last_unit[m] // PAIR + 1)

        def load_quadrants(eng, n, quadrants):
            i, j = plan.loads[n][:2]
            for q in quadrants:
                to = A[plan.slots[n]][Q * q:Q * (q + 1), :]
                if far(n):
                    to, of = to.rearrange("r (t c) -> r t c", t=SUB), far_v[i, j, q]
                else:
                    to, of = to.rearrange("r (m c) -> r m c", m=M), block_v[i, j, q]
                eng.dma_start(to, of).then_inc(block_in[plan.slots[n]], 16)

        def by_node(rows):
            return rows.rearrange("f (q t c) -> f q t c", q=NQ, t=SUB)

        def nodes_in(eng, to, g, signal):
            for q in range(NQ):
                eng.dma_start(to[Q * q:Q * (q + 1)], x_v[g, q]).then_inc(signal, 16)

        block = ctx.enter_context(nc.Block())

        @block.sync
        def _(sp):
            sp.dma_start(w_rows[:], w[:, :]).then_inc(w_in, 16)
            nodes_in(sp, xg, 0, x_in)
            for n, (i, j, summed, used) in enumerate(plan.loads):
                if summed and n % G == G // 2 and n // G + 1 < G:
                    g = n // G + 1
                    sp.wait_ge(h_ready, g)
                    nodes_in(sp, xg, g, x_in)
                block_free(sp, n)
                load_quadrants(sp, n, (0, 1))

        @block.gpsimd
        def _(pool):
            nc.gpsimd.memset(ident[:], 0.0).then_inc(consts_ready, 1)
            pool.wait_ge(consts_ready, 1)
            nc.gpsimd.affine_select(out=ident[:], in_=ident[:], compare_op=ALU.not_equal, fill=1.0, base=0,
                                    pattern=[[-1, P]], channel_multiplier=1).then_inc(ident_ready, 1)
            nc.gpsimd.memset(minus_half[:], -0.5).then_inc(consts_ready, 1)
            pool.wait_ge(ident_ready, 1)
            pool.wait_ge(consts_ready, 2)
            fins = 0
            for e in timeline:
                if e[0] == "sum" and plan.loads[e[1]][0] == plan.loads[e[1]][1]:
                    n, t = e[1:]
                    block_there(pool, n)
                    tile = A[plan.slots[n]][:].rearrange("p (q t c) -> p q t c", q=NQ, t=SUB)[
                        :, :, t, Q * t:Q * (t + 1)]
                    nc.gpsimd.tensor_tensor(out=tile, in0=tile, in1=ident[:].rearrange("p (q c) -> p q c", q=NQ),
                                            op=ALU.add).then_inc(eye_added, 1)
                elif e[0] == "normalise":
                    g = e[1]
                    pool.wait_ge(var_ready, g + 1)
                    if g >= 1:
                        pool.wait_ge(h_ready, g)
                    nc.gpsimd.tensor_tensor(out=rstd[:], in0=variance[:], in1=minus_half[:],
                                            op=ALU.pow).then_inc(rstd_ready, 1)
                    pool.wait_ge(rstd_ready, g + 1)
                    nc.gpsimd.tensor_tensor(out=shift[:], in0=minus_mean[:], in1=rstd[:],
                                            op=ALU.mult).then_inc(shift_ready, 1)
                elif e[0] == "scale":
                    g = e[1]
                    pool.wait_ge(degree_ready, g + 1)
                    nc.gpsimd.tensor_tensor(out=factor[:, g, :], in0=degree[:, g, :], in1=minus_half[:],
                                            op=ALU.pow).then_inc(factor_ready, 1)
                    pool.wait_ge(factor_ready, g + 1)
                    pool.wait_ge(h_ready, g + 1)
                    nc.gpsimd.tensor_tensor(out=S[:, g], in0=S[:, g],
                                            in1=factor[:, g, :].unsqueeze(2).broadcast_to([P, SUB, D]),
                                            op=ALU.mult).then_inc(s_ready, 1)
                elif e[0] == "finish":
                    pool.wait_ge(relu_ready, fins + 1)
                    pool.wait_ge(x_out_in[fins % 2], 16 * NQ * (fins // 2 + 1))
                    nc.gpsimd.tensor_tensor(out=fin[fins % 2][:], in0=fin[fins % 2][:], in1=x_out[fins % 2][:],
                                            op=ALU.add).then_inc(fin_ready, 1)
                    fins += 1

        @block.scalar
        def _(act):
            act.wait_ge(wT_made, 1)
            nc.scalar.copy(wT[:], aux[:, 0:P]).then_inc(wT_ready, 1)
            projects = fins = stores = 0
            for e in timeline:
                if e[0] == "fetch":
                    block_free(act, e[1])
                    load_quadrants(act, e[1], (2, 3))
                elif e[0] == "sum" and on_act(*e[1:]):
                    n, s = e[1:]
                    i, j = plan.loads[n][:2]
                    block_there(act, n)
                    if i == j:
                        act.wait_ge(eye_added, SUB * (i + 1))
                    if i >= 2:
                        act.wait_ge(degree_ready, i - 1)
                    no = act_sum_no[n, s]
                    if no > 2:
                        act.wait_ge(act_summed, no - 2)
                    if far(n):
                        nc.scalar.activation(junk[:, no % 2, :], A[plan.slots[n]][:, s * B:(s + 1) * B], ACT.Copy,
                                             accum_out=far_sums[:, i % 2, s, j:j + 1]).then_inc(act_summed, 1)
                    else:
                        for m in range(SUB * s, SUB * (s + 1)):
                            last = nc.scalar.activation(
                                junk[:, no % 2, m % SUB * P:(m % SUB + 1) * P],
                                A[plan.slots[n]][:, m * P:(m + 1) * P], ACT.Copy,
                                accum_out=near_sums[:, i % 2, j, m:m + 1])
                        last.then_inc(act_summed, 1)
                elif e[0] == "park":
                    i = e[1]
                    act.wait_ge(multiplied, row_end[i, True] + 1)
                    nc.scalar.copy(parked[:, i, :], acc[bank[i, True]][:]).then_inc(parked_ready, 1)
                elif e[0] == "hidden":
                    g = e[1]
                    act.wait_ge(shift_ready, g + 1)
                    for s in range(SUB):
                        last = nc.scalar.activation(S[:, g, s, :], xg[:, s, :], ACT.Relu, bias=shift[:, s:s + 1],
                                                    scale=rstd[:, s:s + 1])
                    last.then_inc(h_ready, 1)
                elif e[0] == "project":
                    if projects == 0:
                        act.wait_ge(h_ready, G)
                    if projects >= 2:
                        act.wait_ge(fin_ready, projects - 1)
                    nodes_in(act, x_out[projects % 2], e[1], x_out_in[projects % 2])
                    projects += 1
                elif e[0] == "finish":
                    i = e[1]
                    act.wait_ge(projected, fins + 1)
                    if fins >= 2:
                        act.wait_ge(stored[fins % 2], 16 * NQ * (fins // 2))
                    for s in range(SUB):
                        last = nc.scalar.activation(fin[fins % 2][:, s, :], aux[:, s * D:(s + 1) * D], ACT.Relu,
                                                    scale=factor[:, i, s:s + 1])
                    last.then_inc(relu_ready, 1)
                    fins += 1
                elif e[0] == "store":
                    act.wait_ge(fin_ready, stores + 1)
                    for q in range(NQ):
                        act.dma_start(out_v[e[1], q], fin[stores % 2][Q * q:Q * (q + 1)]).then_inc(
                            stored[stores % 2], 16)
                    stores += 1
            for r in range(2):
                act.wait_ge(stored[r], 16 * NQ * ((G + 1 - r) // 2))

        @block.vector
        def _(dve):
            dve.wait_ge(ident_ready, 1)
            nc.vector.tensor_reduce(same_row[:], ident[:].rearrange("p (q c) -> p c q", q=NQ), AXX,
                                    ALU.add).then_inc(same_row_ready, 1)
            fins = 0
            for e in timeline:
                if e[0] == "unit":
                    k = e[1]
                    n, i, j, t = units[k]
                    if t % PAIR:
                        continue
                    block_there(dve, n)
                    if i == j:
                        dve.wait_ge(eye_added, SUB * (i + 1))
                    if k >= PAIR * NAT:
                        dve.wait_ge(multiplied, k - PAIR * NAT + PAIR)
                    nc.vector.transpose(AT[k // PAIR % NAT][:].rearrange("p t (m r) -> p t m r", m=M),
                                        A[plan.slots[n]][:].rearrange("p (m t c) -> p t m c", m=M, t=SUB)[
                                            :, t:t + PAIR]).then_inc(pair_ready, 1)
                elif e[0] == "sum" and not on_act(*e[1:]):
                    n, s = e[1:]
                    i, j = plan.loads[n][:2]
                    block_there(dve, n)
                    if i == j:
                        dve.wait_ge(eye_added, SUB * (i + 1))
                    nc.vector.tensor_reduce(near_sums[:, i % 2, j, SUB * s:SUB * (s + 1)],
                                            A[plan.slots[n]][:, s * B:(s + 1) * B].rearrange(
                                                "p (m c) -> p m c", m=SUB),
                                            AXX, ALU.add).then_inc(dve_summed, 1)
                elif e[0] == "normalise":
                    g = e[1]
                    dve.wait_ge(x_in, 16 * NQ * (g + 1))
                    if g >= 1:
                        dve.wait_ge(h_ready, g)
                    for s in range(SUB):
                        last = nc.vector.bn_stats(stats[:, s, :], xg[:, s, :])
                    last.then_inc(stats_ready, 1)
                    dve.wait_ge(stats_ready, g + 1)
                    for s in range(SUB):
                        last = nc.vector.bn_aggr(moments[:, s, :], stats[:, s, :])
                    last.then_inc(moments_ready, 1)
                    dve.wait_ge(moments_ready, g + 1)
                    nc.vector.tensor_scalar(minus_mean[:], moments[:, :, 0], -1.0, None, ALU.mult)
                    nc.vector.tensor_scalar(variance[:], moments[:, :, 1], EPS, None, ALU.add).then_inc(var_ready, 1)
                elif e[0] == "fold":
                    g = e[1]
                    lasts = [n for n in range(len(plan.loads)) if group_of[n] == g and plan.loads[n][2]]
                    dve.wait_ge(act_summed, max(act_sums_by.get(n, 0) for n in lasts))
                    dve.wait_ge(dve_summed, max(dve_sums_by.get(n, 0) for n in lasts))
                    if g >= 1:
                        dve.wait_ge(folded, g)
                    ends = last_held(g, G) + 1
                    if ends < G:
                        nc.vector.tensor_reduce(far_sum[:], far_sums[:, g % 2, :, ends:G], AXX, ALU.add)
                    nc.vector.tensor_reduce(near_sum[:], near_sums[:, g % 2, 0:ends, :].rearrange("p j m -> p m j"),
                                            AXX, ALU.add).then_inc(near_sum_ready, 1)
                elif e[0] == "scale":
                    g = e[1]
                    dve.wait_ge(folded, g + 1)
                    if last_held(g, G) + 1 < G:
                        nc.vector.tensor_tensor(out=degree[:, g, :], in0=fold[:, 0:SUB], in1=far_sum[:],
                                                op=ALU.add).then_inc(degree_ready, 1)
                    else:
                        nc.vector.tensor_copy(degree[:, g, :], fold[:, 0:SUB]).then_inc(degree_ready, 1)
                elif e[0] == "gather":
                    i = e[1]
                    nodes = total[:].rearrange("f (t q c) -> f q t c", q=NQ, t=SUB)
                    if fins >= 1:
                        dve.wait_ge(projected, fins)
                    if i in read_again:
                        dve.wait_ge(multiplied, row_end[i, False] + 1)
                        dve.wait_ge(parked_ready, parks.index(i) + 1)
                        nc.vector.tensor_tensor(out=nodes, in0=by_node(acc[bank[i, False]][:]),
                                                in1=by_node(parked[:, i, :]), op=ALU.add).then_inc(total_ready, 1)
                    else:
                        dve.wait_ge(multiplied, row_end[i, True] + 1)
                        nc.vector.tensor_copy(nodes, by_node(acc[bank[i, True]][:])).then_inc(total_ready, 1)
                    fins += 1

        @block.tensor
        def _(pe):
            pe.wait_ge(w_in, 16)
            pe.wait_ge(ident_ready, 1)
            nc.tensor.transpose(aux[:, 0:P], w_rows[:], ident[:]).then_inc(wT_made, 1)
            fins = 0
            for e in timeline:
                if e[0] == "unit":
                    k = e[1]
                    n, i, j, t = units[k]
                    row = i, plan.loads[n][2]
                    if k == starts[row] and emptied_by[row]:
                        what, former = emptied_by[row]
                        if what == "park":
                            pe.wait_ge(parked_ready, parks.index(former) + 1)
                        else:
                            pe.wait_ge(total_ready, gathers.index(former) + 1)
                    if t == 0:
                        pe.wait_ge(s_ready, j + 1)
                    pe.wait_ge(pair_ready, k // PAIR + 1)
                    nc.tensor.matmul(acc[bank[row]][:], S[:, j, t, :], AT[k // PAIR % NAT][:, k % PAIR],
                                     start=k == starts[row], stop=k == row_end[row]).then_inc(multiplied, 1)
                elif e[0] == "fold":
                    g = e[1]
                    pe.wait_ge(near_sum_ready, g + 1)
                    pe.wait_ge(same_row_ready, 1)
                    for q in range(NQ):
                        last = nc.tensor.matmul(fold[Q * q:Q * (q + 1), 0:SUB], same_row[:],
                                                near_sum[:, SUB * q:SUB * (q + 1)], start=True, stop=True)
                    last.then_inc(folded, 1)
                elif e[0] == "project":
                    pe.wait_ge(total_ready, fins + 1)
                    if fins == 0:
                        pe.wait_ge(wT_ready, 1)
                    else:
                        pe.wait_ge(relu_ready, fins)
                    for s in range(SUB):
                        last = nc.tensor.matmul(aux[:, s * D:(s + 1) * D], total[:, s * P:(s + 1) * P], wT[:],
                                                start=True, stop=True)
                    last.then_inc(projected, 1)
                    fins += 1


def kernel(x, adj, L0_gnn_W):
    import numpy as np
    import concourse.bacc as bacc
    from concourse.bass_utils import run_bass_kernel_spmd

    nc = bacc.Bacc("TRN2", target_bir_lowering=False, num_devices=1, dynamic_dma_scratch_size=1024)
    arrays = {"x": np.ascontiguousarray(x), "adj": np.ascontiguousarray(adj), "w": np.ascontiguousarray(L0_gnn_W)}
    aps = [nc.dram_tensor(n, a.shape, mybir.dt.from_np(a.dtype), kind="ExternalInput").ap() for n, a in arrays.items()]
    out = nc.dram_tensor("out", arrays["x"].shape, F32, kind="ExternalOutput").ap()
    gcn_kernel(nc, *aps, out)
    return run_bass_kernel_spmd(nc, [arrays], core_ids=[0]).results[0]["out"]
```
